# Optimizing a Trainium2 kernel written in Bass

```python
import numpy as np
import jax
import jax.numpy as jnp

def _softmax(x, axis=-1):
    return jax.nn.softmax(x, axis=axis)

def _gelu(x):
    return jax.nn.gelu(x, approximate=True)

def _silu(x):
    return jax.nn.silu(x)

def _sigmoid(x):
    return jax.nn.sigmoid(x)

def _layernorm(x, axis=-1, eps=1e-05):
    m = jnp.mean(x, axis=axis, keepdims=True)
    v = jnp.var(x, axis=axis, keepdims=True)
    return (x - m) / jnp.sqrt(v + eps)

def _scatter_add(tgt, idx, src, axis=0):
    return tgt.at[idx].add(src)

def _segment_sum(src, seg, n):
    return jax.ops.segment_sum(src, seg, n)
kernel_name = 'mk_dlrm_tower_d1_rec_r8_a28f98'

def setup_inputs(seed: int=0):
    np.random.seed(seed)
    _w = jnp.asarray

    def _rec_inputs():
        import jax
        import jax.numpy as jnp
        _tk = jax.random.key(seed)
        ids = jnp.stack([jax.random.randint(jax.random.fold_in(_tk, 200 + f), (512,), 0, v, jnp.int32) for f, v in enumerate([125000, 1000, 1250, 1250, 1250, 1250, 12500, 1000, 12500, 12500, 12500, 12500, 1000, 1250, 1250, 12500, 12500, 1000, 1000, 12500, 1250, 1250, 1000, 1000, 1250, 1250])], axis=1)
        tbl_0 = 0.05 * jax.random.normal(jax.random.fold_in(_tk, 500 + 0), (125000, 128), jnp.float32)
        tbl_1 = 0.05 * jax.random.normal(jax.random.fold_in(_tk, 500 + 1), (1000, 128), jnp.float32)
        tbl_2 = 0.05 * jax.random.normal(jax.random.fold_in(_tk, 500 + 2), (1250, 128), jnp.float32)
        tbl_3 = 0.05 * jax.random.normal(jax.random.fold_in(_tk, 500 + 3), (1250, 128), jnp.float32)
        tbl_4 = 0.05 * jax.random.normal(jax.random.fold_in(_tk, 500 + 4), (1250, 128), jnp.float32)
        tbl_5 = 0.05 * jax.random.normal(jax.random.fold_in(_tk, 500 + 5), (1250, 128), jnp.float32)
        tbl_6 = 0.05 * jax.random.normal(jax.random.fold_in(_tk, 500 + 6), (12500, 128), jnp.float32)
        tbl_7 = 0.05 * jax.random.normal(jax.random.fold_in(_tk, 500 + 7), (1000, 128), jnp.float32)
        tbl_8 = 0.05 * jax.random.normal(jax.random.fold_in(_tk, 500 + 8), (12500, 128), jnp.float32)
        tbl_9 = 0.05 * jax.random.normal(jax.random.fold_in(_tk, 500 + 9), (12500, 128), jnp.float32)
        tbl_10 = 0.05 * jax.random.normal(jax.random.fold_in(_tk, 500 + 10), (12500, 128), jnp.float32)
        tbl_11 = 0.05 * jax.random.normal(jax.random.fold_in(_tk, 500 + 11), (12500, 128), jnp.float32)
        tbl_12 = 0.05 * jax.random.normal(jax.random.fold_in(_tk, 500 + 12), (1000, 128), jnp.float32)
        tbl_13 = 0.05 * jax.random.normal(jax.random.fold_in(_tk, 500 + 13), (1250, 128), jnp.float32)
        tbl_14 = 0.05 * jax.random.normal(jax.random.fold_in(_tk, 500 + 14), (1250, 128), jnp.float32)
        tbl_15 = 0.05 * jax.random.normal(jax.random.fold_in(_tk, 500 + 15), (12500, 128), jnp.float32)
        tbl_16 = 0.05 * jax.random.normal(jax.random.fold_in(_tk, 500 + 16), (12500, 128), jnp.float32)
        tbl_17 = 0.05 * jax.random.normal(jax.random.fold_in(_tk, 500 + 17), (1000, 128), jnp.float32)
        tbl_18 = 0.05 * jax.random.normal(jax.random.fold_in(_tk, 500 + 18), (1000, 128), jnp.float32)
        tbl_19 = 0.05 * jax.random.normal(jax.random.fold_in(_tk, 500 + 19), (12500, 128), jnp.float32)
        tbl_20 = 0.05 * jax.random.normal(jax.random.fold_in(_tk, 500 + 20), (1250, 128), jnp.float32)
        tbl_21 = 0.05 * jax.random.normal(jax.random.fold_in(_tk, 500 + 21), (1250, 128), jnp.float32)
        tbl_22 = 0.05 * jax.random.normal(jax.random.fold_in(_tk, 500 + 22), (1000, 128), jnp.float32)
        tbl_23 = 0.05 * jax.random.normal(jax.random.fold_in(_tk, 500 + 23), (1000, 128), jnp.float32)
        tbl_24 = 0.05 * jax.random.normal(jax.random.fold_in(_tk, 500 + 24), (1250, 128), jnp.float32)
        tbl_25 = 0.05 * jax.random.normal(jax.random.fold_in(_tk, 500 + 25), (1250, 128), jnp.float32)
        _rk = jax.random.fold_in(_tk, 7)
        r_dense_x = -0.000514642 + 1.00011 * jax.random.normal(jax.random.fold_in(_rk, 101), (512, 128), jnp.float32)
        W_top1 = 0.0456912 * jax.random.normal(jax.random.fold_in(_tk, 801), (479, 512), jnp.float32)
        W_top2 = 0.0441942 * jax.random.normal(jax.random.fold_in(_tk, 802), (512, 256), jnp.float32)
        W_top3 = 0.0625 * jax.random.normal(jax.random.fold_in(_tk, 803), (256, 1), jnp.float32)
        b_top1 = jnp.zeros((512,), jnp.float32)
        b_top2 = jnp.zeros((256,), jnp.float32)
        return (r_dense_x, ids, tbl_0, tbl_1, tbl_2, tbl_3, tbl_4, tbl_5, tbl_6, tbl_7, tbl_8, tbl_9, tbl_10, tbl_11, tbl_12, tbl_13, tbl_14, tbl_15, tbl_16, tbl_17, tbl_18, tbl_19, tbl_20, tbl_21, tbl_22, tbl_23, tbl_24, tbl_25, W_top1, b_top1, W_top2, b_top2, W_top3)
    r_dense_x, ids, tbl_0, tbl_1, tbl_2, tbl_3, tbl_4, tbl_5, tbl_6, tbl_7, tbl_8, tbl_9, tbl_10, tbl_11, tbl_12, tbl_13, tbl_14, tbl_15, tbl_16, tbl_17, tbl_18, tbl_19, tbl_20, tbl_21, tbl_22, tbl_23, tbl_24, tbl_25, W_top1, b_top1, W_top2, b_top2, W_top3 = _rec_inputs()

    def _L0_rec_setup():
        import jax, jax.numpy as jnp
        import numpy as np
        F = 26
        D = 128
        B = 2048
        _TRIU_I, _TRIU_J = np.triu_indices(F + 1, k=1)
        _TRIU_I = jnp.asarray(_TRIU_I)
        _TRIU_J = jnp.asarray(_TRIU_J)
        key = jax.random.key(seed)
        k1, k2 = jax.random.split(key)
        sparse_x = jax.random.normal(k1, (B, F, D), dtype=jnp.float32)
        dense_x = jax.random.normal(k2, (B, D), dtype=jnp.float32)
        return {'sparse_x': sparse_x, 'dense_x': dense_x}
    _L0_rec_all = _L0_rec_setup()
    _L0_rec_in = {k: v for k, v in _L0_rec_all.items() if k in ()}
    del _L0_rec_all
    return {'r_dense_x': r_dense_x, 'ids': ids, 'tbl_0': tbl_0, 'tbl_1': tbl_1, 'tbl_2': tbl_2, 'tbl_3': tbl_3, 'tbl_4': tbl_4, 'tbl_5': tbl_5, 'tbl_6': tbl_6, 'tbl_7': tbl_7, 'tbl_8': tbl_8, 'tbl_9': tbl_9, 'tbl_10': tbl_10, 'tbl_11': tbl_11, 'tbl_12': tbl_12, 'tbl_13': tbl_13, 'tbl_14': tbl_14, 'tbl_15': tbl_15, 'tbl_16': tbl_16, 'tbl_17': tbl_17, 'tbl_18': tbl_18, 'tbl_19': tbl_19, 'tbl_20': tbl_20, 'tbl_21': tbl_21, 'tbl_22': tbl_22, 'tbl_23': tbl_23, 'tbl_24': tbl_24, 'tbl_25': tbl_25, 'W_top1': W_top1, 'b_top1': b_top1, 'W_top2': W_top2, 'b_top2': b_top2, 'W_top3': W_top3}

def reference(r_dense_x, ids, tbl_0, tbl_1, tbl_2, tbl_3, tbl_4, tbl_5, tbl_6, tbl_7, tbl_8, tbl_9, tbl_10, tbl_11, tbl_12, tbl_13, tbl_14, tbl_15, tbl_16, tbl_17, tbl_18, tbl_19, tbl_20, tbl_21, tbl_22, tbl_23, tbl_24, tbl_25, W_top1, b_top1, W_top2, b_top2, W_top3):
    import jax
    import jax.numpy as jnp

    def _L0_rec_ref(sparse_x, dense_x):
        import jax, jax.numpy as jnp
        import numpy as np
        F = 26
        D = 128
        B = 2048
        _TRIU_I, _TRIU_J = np.triu_indices(F + 1, k=1)
        _TRIU_I = jnp.asarray(_TRIU_I)
        _TRIU_J = jnp.asarray(_TRIU_J)
        combined = jnp.concatenate([sparse_x, dense_x[:, None, :]], axis=1)
        interact = jnp.einsum('bfd,bgd->bfg', combined, combined)
        return interact[:, _TRIU_I, _TRIU_J]
    e = jnp.stack([tbl_0[ids[:, 0]], tbl_1[ids[:, 1]], tbl_2[ids[:, 2]], tbl_3[ids[:, 3]], tbl_4[ids[:, 4]], tbl_5[ids[:, 5]], tbl_6[ids[:, 6]], tbl_7[ids[:, 7]], tbl_8[ids[:, 8]], tbl_9[ids[:, 9]], tbl_10[ids[:, 10]], tbl_11[ids[:, 11]], tbl_12[ids[:, 12]], tbl_13[ids[:, 13]], tbl_14[ids[:, 14]], tbl_15[ids[:, 15]], tbl_16[ids[:, 16]], tbl_17[ids[:, 17]], tbl_18[ids[:, 18]], tbl_19[ids[:, 19]], tbl_20[ids[:, 20]], tbl_21[ids[:, 21]], tbl_22[ids[:, 22]], tbl_23[ids[:, 23]], tbl_24[ids[:, 24]], tbl_25[ids[:, 25]]], axis=1)
    z = _L0_rec_ref(e, r_dense_x)
    z = z.reshape(z.shape[0], -1)
    h = jnp.concatenate([z, r_dense_x], axis=1)
    h = jnp.maximum(h @ W_top1 + b_top1, 0.0)
    h = jnp.maximum(h @ W_top2 + b_top2, 0.0)
    y = h @ W_top3
    return y

_drawn_inputs = setup_inputs


def setup_inputs(seed=0):
    import zlib

    import numpy as np

    out = dict(_drawn_inputs(seed))
    spreads = {'b_top1': (0.0, 0.1), 'b_top2': (0.0, 0.1)}
    factors = {}
    for name, (base, spread) in spreads.items():
        noise = np.random.default_rng([zlib.crc32(name.encode()), seed]).standard_normal(out[name].shape)
        drawn = base * np.exp(spread * noise) if base else spread * noise
        out[name] = jnp.asarray(drawn.astype(out[name].dtype))
    for name, factor in factors.items():
        out[name] = (out[name] * factor).astype(out[name].dtype)
    return out
```

```python
import concourse.bass as bass
from concourse import mybir
from contextlib import ExitStack

B, D, P = 512, 128, 128
TILES = B // P
FEATURES = 26
DENSE = FEATURES
SLOTS = FEATURES + 1
PAIRS = SLOTS * (SLOTS - 1) // 2
H1, H2 = 512, 256
ROWS = [125000, 1000, 1250, 1250, 1250, 1250, 12500, 1000, 12500, 12500, 12500, 12500, 1000,
        1250, 1250, 12500, 12500, 1000, 1000, 12500, 1250, 1250, 1000, 1000, 1250, 1250]
ONE_HOT = [1, 7, 12, 17, 18, 22, 23, 2]
GATHERED = [f for f in range(FEATURES) if f not in ONE_HOT]
ORDER = GATHERED + ONE_HOT + [DENSE]
N_HOT, N_GATHERED = len(ONE_HOT), len(GATHERED)
ROW_PARTS = 125
CHUNKS = [ROWS[f] // ROW_PARTS for f in ONE_HOT]
MAX_CHUNKS = max(CHUNKS)
QUAD = 32
QUADS = P // QUAD
COLS = SLOTS - 1
QCOLS = -(-COLS // QUADS)
BANK = 512
GROUP = 4
BANK_GROUPS = 4
DOT_BANKS = QUAD // BANK_GROUPS
HOT_RING, TABLE_RING, IDB_RING, W_RING, GATHER_RING = 8, 2, 3, 2, 2
W_CHUNKS = QCOLS + 1


def quad_cols(q):
    return min(QCOLS, COLS - q * QCOLS)


def plan():
    banks = [(t, s) for t in range(TILES) for s in range(0, N_GATHERED, GROUP)]
    steps = []
    for i in range(N_HOT):
        steps += [("hot", i), ("weights", i)]
        if i >= 1:
            steps.append(("transpose", *banks.pop(0)))
    for c in range(N_HOT, W_CHUNKS):
        steps.append(("weights", c))
    for t in range(TILES):
        while banks and banks[0][0] == t:
            steps.append(("transpose", *banks.pop(0)))
        steps.append(("dots", t))
        if banks:
            steps.append(("transpose", *banks.pop(0)))
        steps += [("layer1", t), ("layer2", t)]
    return steps


def dlrm_kernel(nc, ids, hot_ids, dense_t, tables, w_pairs, w_dense, w2, b2, w3, out):
    f32, f32r, i32 = mybir.dt.float32, mybir.dt.float32r, mybir.dt.int32
    ALU, ACT = mybir.AluOpType, mybir.ActivationFunctionType
    STEPS = plan()

    with ExitStack() as ctx:
        def sb(name, shape, dt=f32):
            return ctx.enter_context(nc.sbuf_tensor(name, shape, dt))

        def pb(name):
            return ctx.enter_context(nc.psum_tensor(name, [P, BANK], f32))

        def sem(name):
            return ctx.enter_context(nc.semaphore(name))

        idx = sb("idx", [P, TILES * FEATURES], i32)
        n_raw, n_dots = TABLE_RING * MAX_CHUNKS * D, QUADS * COLS * QUAD
        shared = sb("shared", [P, max(n_raw + IDB_RING * B, n_dots)])
        table_raw = shared[0:ROW_PARTS, 0:n_raw].rearrange("p (r n) -> p r n", r=TABLE_RING)
        hot_ids_b = shared[0:ROW_PARTS, n_raw:n_raw + IDB_RING * B].bitcast(i32).rearrange(
            "p (r b) -> p r b", r=IDB_RING)
        dots = shared[:, 0:n_dots].rearrange("p (j g k) -> p j g k", j=QUADS, g=COLS)
        row_numbers = {c: sb(f"row_numbers{c}", [ROW_PARTS, c]) for c in sorted(set(CHUNKS))}
        table_hi = sb("table_hi", [ROW_PARTS, TABLE_RING, MAX_CHUNKS * D], f32r)
        table_lo = sb("table_lo", [ROW_PARTS, TABLE_RING, MAX_CHUNKS * D], f32r)
        one_hot = sb("one_hot", [ROW_PARTS, HOT_RING, B], f32r)
        gathered = sb("gathered", [P, GATHER_RING, N_GATHERED, D])
        combined_t = sb("combined_t", [P, TILES, QUAD, QUADS, QUAD])
        x_t = sb("x_t", [P, B])
        x_hi = sb("x_hi", [P, B], f32r)
        x_lo = sb("x_lo", [P, B], f32r)
        pairs = sb("pairs", [P, 2, QUADS, QCOLS, QUAD])
        pairs_hi = sb("pairs_hi", [P, QCOLS, P], f32r)
        pairs_lo = sb("pairs_lo", [P, QCOLS, P], f32r)
        w1_raw = sb("w1_raw", [P, W_RING, H1])
        w1_hi = sb("w1_hi", [P, W_CHUNKS, H1], f32r)
        w1_lo = sb("w1_lo", [P, W_CHUNKS, H1], f32r)
        w2_sb = sb("w2_sb", [P, H1 // P, H2])
        b2_b = sb("b2_b", [P, H2])
        w3_b = sb("w3_b", [P, H2])
        h1 = sb("h1", [P, H1])
        h1_t = sb("h1_t", [P, H1])
        h2 = sb("h2", [P, H2])
        h2_w3 = sb("h2_w3", [P, H2])
        y = sb("y", [P, TILES])
        ident = sb("ident", [P, P])

        slot_banks = [pb(f"slot_bank{i}") for i in range(2)]
        dot_banks = [pb(f"dot_bank{i}") for i in range(3)]
        h_bank = pb("h_bank")
        ht_bank = pb("ht_bank")

        ids_in, x_in, w2_in, b2_in, w3_in = (sem(n) for n in ("ids_in", "x_in", "w2_in", "b2_in", "w3_in"))
        hot_ids_in = [sem(f"hot_ids_in{i}") for i in range(IDB_RING)]
        table_in = [sem(f"table_in{i}") for i in range(TABLE_RING)]
        w1_in = [sem(f"w1_in{i}") for i in range(W_RING)]
        n_banks = -(-N_GATHERED // GROUP)
        rows_in = [[sem(f"rows_in{r}_{g}") for g in range(n_banks)] for r in range(GATHER_RING)]
        shuffled = [sem(f"shuffled{i}") for i in range(2)]
        y_out = sem("y_out")
        ident_zero, ident_done, rows_numbered = sem("ident_zero"), sem("ident_done"), sem("rows_numbered")
        pads_done = sem("pads_done")
        table_hi_done, table_lo_done = sem("table_hi_done"), sem("table_lo_done")
        hot_built, hot_used = sem("hot_built"), sem("hot_used")
        transposed, slot_bank_free = sem("transposed"), sem("slot_bank_free")
        x_hi_done, x_lo_done, x_slot_done = sem("x_hi_done"), sem("x_lo_done"), sem("x_slot_done")
        w1_hi_done, w1_lo_done = sem("w1_hi_done"), sem("w1_lo_done")
        dot_bank_full = sem("dot_bank_full")
        dots_even, dots_odd = sem("dots_even"), sem("dots_odd")
        pairs_hi_done, pairs_lo_done = sem("pairs_hi_done"), sem("pairs_lo_done")
        h1_full, h1_done, h1t_full, h1t_done = sem("h1_full"), sem("h1_done"), sem("h1t_full"), sem("h1t_done")
        h2_full, h2_done, h2_relu, y_done = sem("h2_full"), sem("h2_done"), sem("h2_relu"), sem("y_done")

        block = ctx.enter_context(nc.Block())

        def hot_slot(i):
            return combined_t[:, :, :, :, i].rearrange("p t k j -> p t j k")

        def by_batch(ap):
            return ap.rearrange("p (t j k) -> p t j k", t=TILES, j=QUADS)

        bank_no, banks_before, k = {}, {}, 0
        for step in STEPS:
            if step[0] in ("hot", "transpose"):
                bank_no[step] = k
                k += 1
            elif step[0] == "dots":
                banks_before[step[1]] = k
        hot_before = [sum(CHUNKS[:i]) for i in range(N_HOT + 1)]
        DOT_RING = len(dot_banks)

        def dots_emptied(eng, n):
            eng.wait_ge(dots_even, (n + 1) // 2)
            if n >= 2:
                eng.wait_ge(dots_odd, n // 2)

        @block.sync
        def _(sp):
            sp.dma_start(idx[:], ids).then_inc(ids_in, 16)

            def load_hot(i):
                if i >= IDB_RING:
                    sp.wait_ge(hot_built, hot_before[i - IDB_RING + 1])
                sp.dma_start(hot_ids_b[:, i % IDB_RING, :],
                             hot_ids[i:i + 1, :].partition_broadcast(ROW_PARTS).rearrange("p o b -> p (o b)")
                             ).then_inc(hot_ids_in[i % IDB_RING], 16)
                if i >= TABLE_RING:
                    sp.wait_ge(table_lo_done, i - TABLE_RING + 1)
                n = CHUNKS[i] * D
                src = tables[ONE_HOT[i]].rearrange("(p c) d -> p (c d)", p=ROW_PARTS)
                for lo, hi in ((0, 112), (112, ROW_PARTS)):
                    sp.dma_start(table_raw[lo:hi, i % TABLE_RING, 0:n], src[lo:hi, :]
                                 ).then_inc(table_in[i % TABLE_RING], 16)

            def load_w1(c):
                if c >= W_RING:
                    sp.wait_ge(w1_lo_done, c - W_RING + 1)
                src = w_pairs[:, c * H1:(c + 1) * H1] if c < QCOLS else w_dense
                sp.dma_start(w1_raw[:, c % W_RING, :], src).then_inc(w1_in[c % W_RING], 16)

            for i in range(TABLE_RING):
                load_hot(i)
            sp.dma_start(x_t[:], dense_t).then_inc(x_in, 16)
            load_w1(0)
            load_w1(1)
            for i in range(TABLE_RING, N_HOT):
                load_hot(i)
                if i < W_CHUNKS:
                    load_w1(i)
            for c in range(N_HOT, W_CHUNKS):
                load_w1(c)
            sp.dma_start(w2_sb[:], w2.rearrange("(c p) n -> p c n", p=P)).then_inc(w2_in, 16)
            sp.dma_start(b2_b[:], b2.partition_broadcast(P).rearrange("p o n -> p (o n)")).then_inc(b2_in, 16)
            sp.dma_start(w3_b[:], w3.partition_broadcast(P).rearrange("p o n -> p (o n)")).then_inc(w3_in, 16)

            for t in range(TILES):
                dots_emptied(sp, DOT_BANKS * (t + 1))
                if t == 0:
                    sp.wait_ge(pads_done, 3)
                if t >= 2:
                    sp.wait_ge(pairs_hi_done, t - 1)
                    sp.wait_ge(pairs_lo_done, t - 1)
                for j in range(QUADS):
                    for q in range(QUADS):
                        n = quad_cols(q)
                        sp.dma_start(pairs[q * QUAD:q * QUAD + SLOTS, t % 2, j, 0:n, :],
                                     dots[j * QUAD:j * QUAD + SLOTS, j, q * QCOLS:q * QCOLS + n, :]
                                     ).then_inc(shuffled[t % 2], 16)
                if t >= 1:
                    sp.wait_ge(y_done, t)
                    sp.dma_start(out[(t - 1) * P:t * P, :], y[:, t - 1:t]).then_inc(y_out, 16)
            sp.wait_ge(y_done, TILES)
            sp.dma_start(out[(TILES - 1) * P:B, :], y[:, TILES - 1:TILES]).then_inc(y_out, 16)
            sp.wait_ge(y_out, 16 * TILES)

        @block.gpsimd
        def _(pool):
            for c in row_numbers:
                pool.iota(row_numbers[c][:], pattern=[[1, c]], base=0, channel_multiplier=c,
                          allow_small_or_imprecise_dtypes=True).then_inc(rows_numbered, 1)
            pool.memset(ident[:], 0.0).then_inc(ident_zero, 1)
            pool.wait_ge(ident_zero, 1)
            pool.affine_select(out=ident[:], in_=ident[:], compare_op=ALU.not_equal, fill=1.0,
                               base=0, pattern=[[-1, P]], channel_multiplier=1).then_inc(ident_done, 1)
            pool.wait_ge(ids_in, 16)
            for t in range(TILES):
                for n, f in enumerate(GATHERED):
                    if t >= GATHER_RING and n % GROUP == 0:
                        pool.wait_ge(transposed, (t - GATHER_RING) * n_banks + n // GROUP + 1)
                    pool.indirect_dma_start(
                        gathered[:, t % GATHER_RING, n, :], None, tables[f],
                        bass.IndirectOffsetOnAxis(ap=idx[:, t * FEATURES + f:t * FEATURES + f + 1], axis=0)
                    ).then_inc(rows_in[t % GATHER_RING][n // GROUP], 16)

        @block.scalar
        def _(act):
            def split_table(i):
                act.wait_ge(table_in[i % TABLE_RING], 32 * (i // TABLE_RING + 1))
                if i >= TABLE_RING:
                    act.wait_ge(hot_used, hot_before[i - TABLE_RING + 1])
                n = CHUNKS[i] * D
                act.activation(table_hi[:, i % TABLE_RING, 0:n], table_raw[:, i % TABLE_RING, 0:n],
                               ACT.Copy).then_inc(table_hi_done, 1)

            for i in range(TABLE_RING):
                split_table(i)
            act.wait_ge(x_in, 16)
            act.activation(x_hi[:], x_t[:], ACT.Copy).then_inc(x_hi_done, 1)
            act.activation(hot_slot(SLOTS - 1), by_batch(x_t[:]),
                           ACT.Copy).then_inc(x_slot_done, 1)

            for step in STEPS:
                kind, i = step[0], step[1]
                if kind == "hot":
                    n = bank_no[step]
                    act.wait_ge(hot_used, hot_before[i + 1])
                    act.activation(hot_slot(N_GATHERED + i),
                                   by_batch(slot_banks[n % 2][:]),
                                   ACT.Copy).then_inc(slot_bank_free, 1)
                    if i + TABLE_RING < N_HOT:
                        split_table(i + TABLE_RING)
                elif kind == "weights":
                    if i < W_CHUNKS:
                        act.wait_ge(w1_in[i % W_RING], 16 * (i // W_RING + 1))
                        act.activation(w1_hi[:, i, :], w1_raw[:, i % W_RING, :], ACT.Copy).then_inc(w1_hi_done, 1)
                elif kind == "transpose":
                    n, s = bank_no[step], step[2]
                    g = min(GROUP, N_GATHERED - s)
                    act.wait_ge(transposed, i * n_banks + s // GROUP + 1)
                    act.activation(combined_t[:, i, :, :, s:s + g].rearrange("p k j g -> p g j k"),
                                   slot_banks[n % 2][:, 0:g * P].rearrange("p (g j k) -> p g j k", g=g, j=QUADS),
                                   ACT.Copy).then_inc(slot_bank_free, 1)
                elif kind == "dots":
                    for m in range(1, DOT_BANKS, 2):
                        n = i * DOT_BANKS + m
                        act.wait_ge(dot_bank_full, n + 1)
                        if i >= 1 and m == 1:
                            act.wait_ge(shuffled[(i - 1) % 2], 16 * QUADS * QUADS * ((i - 1) // 2 + 1))
                        act.activation(
                            dots[:, :, :, m * BANK_GROUPS:(m + 1) * BANK_GROUPS].rearrange("p j g k -> p k j g"),
                            dot_banks[n % DOT_RING][:, 0:BANK_GROUPS * QUADS * COLS].rearrange(
                                "p (k j g) -> p k j g", k=BANK_GROUPS, j=QUADS), ACT.Copy).then_inc(dots_odd, 1)
                elif kind == "layer1":
                    act.wait_ge(shuffled[i % 2], 16 * QUADS * QUADS * (i // 2 + 1))
                    if i >= 1:
                        act.wait_ge(h1_full, i)
                    act.activation(pairs_hi[:].rearrange("p g (j k) -> p j g k", j=QUADS), pairs[:, i % 2],
                                   ACT.Copy).then_inc(pairs_hi_done, 1)
                    act.wait_ge(h1_full, i + 1)
                    if i >= 1:
                        act.wait_ge(h1t_full, i)
                    act.activation(h1[:], h_bank[:], ACT.Relu).then_inc(h1_done, 1)

        @block.vector
        def _(dve):
            dve.memset(combined_t[:, :, :, :, SLOTS:QUAD], 0.0).then_inc(pads_done, 1)
            dve.memset(pairs[:, :, :, 0, :], 1.0).then_inc(pads_done, 1)
            dve.memset(pairs[:, :, :, 1:QCOLS, :], 0.0).then_inc(pads_done, 1)

            def split_table(i):
                dve.wait_ge(table_hi_done, i + 1)
                if i >= TABLE_RING:
                    dve.wait_ge(hot_used, hot_before[i - TABLE_RING + 1])
                n = CHUNKS[i] * D
                dve.tensor_tensor(table_lo[:, i % TABLE_RING, 0:n], table_raw[:, i % TABLE_RING, 0:n],
                                  table_hi[:, i % TABLE_RING, 0:n].bitcast(f32),
                                  ALU.subtract).then_inc(table_lo_done, 1)

            split_table(0)
            dve.wait_ge(rows_numbered, len(row_numbers))
            for step in STEPS:
                kind, i = step[0], step[1]
                if kind == "hot":
                    if i + 1 < N_HOT:
                        split_table(i + 1)
                    dve.wait_ge(hot_ids_in[i % IDB_RING], 16 * (i // IDB_RING + 1))
                    for c in range(CHUNKS[i]):
                        n = hot_before[i] + c
                        if n >= HOT_RING:
                            dve.wait_ge(hot_used, n - HOT_RING + 1)
                        dve.tensor_scalar(one_hot[:, n % HOT_RING, :], hot_ids_b[:, i % IDB_RING, :],
                                          row_numbers[CHUNKS[i]][:, c:c + 1], None,
                                          ALU.is_equal).then_inc(hot_built, 1)
                    if i == 0:
                        dve.wait_ge(x_hi_done, 1)
                        dve.tensor_tensor(x_lo[:], x_t[:], x_hi[:].bitcast(f32), ALU.subtract).then_inc(x_lo_done, 1)
                elif kind == "weights":
                    if i < W_CHUNKS:
                        dve.wait_ge(w1_hi_done, i + 1)
                        dve.tensor_tensor(w1_lo[:, i, :], w1_raw[:, i % W_RING, :], w1_hi[:, i, :].bitcast(f32),
                                          ALU.subtract).then_inc(w1_lo_done, 1)
                elif kind == "dots":
                    for m in range(0, DOT_BANKS, 2):
                        n = i * DOT_BANKS + m
                        dve.wait_ge(dot_bank_full, n + 1)
                        if i >= 1 and m == 0:
                            dve.wait_ge(shuffled[(i - 1) % 2], 16 * QUADS * QUADS * ((i - 1) // 2 + 1))
                        dve.tensor_copy(
                            dots[:, :, :, m * BANK_GROUPS:(m + 1) * BANK_GROUPS].rearrange("p j g k -> p k j g"),
                            dot_banks[n % DOT_RING][:, 0:BANK_GROUPS * QUADS * COLS].rearrange(
                                "p (k j g) -> p k j g", k=BANK_GROUPS, j=QUADS)).then_inc(dots_even, 1)
                elif kind == "layer1":
                    dve.wait_ge(pairs_hi_done, i + 1)
                    dve.tensor_tensor(pairs_lo[:].rearrange("p g (j k) -> p j g k", j=QUADS), pairs[:, i % 2],
                                      pairs_hi[:].bitcast(f32).rearrange("p g (j k) -> p j g k", j=QUADS),
                                      ALU.subtract).then_inc(pairs_lo_done, 1)
                elif kind == "layer2":
                    dve.wait_ge(h1t_full, i + 1)
                    dve.tensor_copy(h1_t[:], ht_bank[:]).then_inc(h1t_done, 1)
                    if i == 0:
                        dve.wait_ge(b2_in, 16)
                        dve.wait_ge(w3_in, 16)
                    dve.wait_ge(h2_full, i + 1)
                    dve.tensor_tensor(h2[:], h_bank[:, 0:H2], b2_b[:], ALU.add).then_inc(h2_done, 1)
                    dve.wait_ge(h2_done, i + 1)
                    dve.scalar_tensor_tensor(out=h2_w3[:], in0=h2[:], scalar=0.0, in1=w3_b[:], op0=ALU.max,
                                             op1=ALU.mult, accum_out=y[:, i:i + 1]).then_inc(y_done, 1)

        @block.tensor
        def _(pe):
            pe.wait_ge(ident_done, 1)
            for step in STEPS:
                kind, i = step[0], step[1]
                if kind in ("hot", "transpose"):
                    n = bank_no[step]
                    bank = slot_banks[n % 2]
                    if n >= 2:
                        pe.wait_ge(slot_bank_free, n - 1)
                if kind == "hot":
                    pe.wait_ge(table_lo_done, i + 1)
                    r = i % TABLE_RING
                    for c in range(CHUNKS[i]):
                        m = hot_before[i] + c
                        pe.wait_ge(hot_built, m + 1)
                        pe.matmul(bank[:], table_hi[:, r, c * D:(c + 1) * D], one_hot[:, m % HOT_RING, :],
                                  start=(c == 0), stop=False)
                        last = pe.matmul(bank[:], table_lo[:, r, c * D:(c + 1) * D], one_hot[:, m % HOT_RING, :],
                                         start=False, stop=(c == CHUNKS[i] - 1))
                        last.then_inc(hot_used, 1)
                elif kind == "transpose":
                    s = step[2]
                    g = min(GROUP, N_GATHERED - s)
                    pe.wait_ge(rows_in[i % GATHER_RING][s // GROUP], 16 * g * (i // GATHER_RING + 1))
                    for m in range(g):
                        last = pe.transpose(bank[:, m * P:(m + 1) * P], gathered[:, i % GATHER_RING, s + m, :], ident[:])
                    last.then_inc(transposed, 1)
                elif kind == "dots":
                    if i == 0:
                        pe.wait_ge(x_slot_done, 1)
                        pe.wait_ge(pads_done, 1)
                    pe.wait_ge(slot_bank_free, banks_before[i])
                    for m in range(DOT_BANKS):
                        n = i * DOT_BANKS + m
                        bank = dot_banks[n % DOT_RING]
                        if n >= DOT_RING:
                            dots_emptied(pe, n - DOT_RING + 1)
                        for g in range(BANK_GROUPS):
                            k = m * BANK_GROUPS + g
                            last = pe.matmul(bank[:, g * QUADS * COLS:(g + 1) * QUADS * COLS],
                                             combined_t[:, i, k].rearrange("p j s -> p (j s)"),
                                             combined_t[:, i, k, :, 1:SLOTS],
                                             start=True, stop=True)
                        last.then_inc(dot_bank_full, 1)
                elif kind == "layer1":
                    if i == 0:
                        pe.wait_ge(x_lo_done, 1)
                        pe.wait_ge(w1_lo_done, W_CHUNKS)
                    else:
                        pe.wait_ge(h2_done, i)
                    parts = [(x_hi[:, i * P:(i + 1) * P], x_lo[:, i * P:(i + 1) * P], QCOLS)]
                    parts += [(pairs_hi[:, c, :], pairs_lo[:, c, :], c) for c in range(QCOLS)]
                    for n, (hi, lo, c) in enumerate(parts):
                        if n == 1:
                            pe.wait_ge(pairs_lo_done, i + 1)
                        pe.matmul(h_bank[:], hi, w1_hi[:, c, :], start=(n == 0), stop=False)
                        pe.matmul(h_bank[:], hi, w1_lo[:, c, :], start=False, stop=False)
                        last = pe.matmul(h_bank[:], lo, w1_hi[:, c, :], start=False, stop=(n == len(parts) - 1))
                    last.then_inc(h1_full, 1)
                elif kind == "layer2":
                    pe.wait_ge(h1_done, i + 1)
                    if i >= 1:
                        pe.wait_ge(h1t_done, i)
                    for c in range(H1 // P):
                        last = pe.transpose(ht_bank[:, c * P:(c + 1) * P], h1[:, c * P:(c + 1) * P], ident[:])
                    last.then_inc(h1t_full, 1)
                    if i == 0:
                        pe.wait_ge(w2_in, 16)
                    pe.wait_ge(h1t_done, i + 1)
                    for c in range(H1 // P):
                        last = pe.matmul(h_bank[:, 0:H2], h1_t[:, c * P:(c + 1) * P], w2_sb[:, c, :],
                                         start=(c == 0), stop=(c == H1 // P - 1))
                    last.then_inc(h2_full, 1)


def pair_row(f, g):
    f, g = min(f, g), max(f, g)
    return f * SLOTS - f * (f + 1) // 2 + g - f - 1


def kernel(**inputs):
    import numpy as np
    import concourse.bacc as bacc
    from concourse.bass_utils import run_bass_kernel_spmd

    a = {name: np.ascontiguousarray(x) for name, x in inputs.items()}
    w_pairs = np.zeros((P, QCOLS, H1), a["W_top1"].dtype)
    for g in range(1, SLOTS):
        q, c = divmod(g - 1, QCOLS)
        for f in range(g):
            w_pairs[q * QUAD + f, c] = a["W_top1"][pair_row(ORDER[f], ORDER[g])]
    w_pairs[SLOTS, 0] = a["b_top1"]
    arrays = {
        "ids": np.ascontiguousarray(a["ids"].reshape(TILES, P, FEATURES).transpose(1, 0, 2).reshape(P, -1)),
        "hot_ids": np.ascontiguousarray(a["ids"].T[ONE_HOT]),
        "dense_t": np.ascontiguousarray(a["r_dense_x"].T),
        "w_pairs": w_pairs.reshape(P, -1),
        "w_dense": np.ascontiguousarray(a["W_top1"][PAIRS:]),
        "w2": a["W_top2"],
        "b2": a["b_top2"].reshape(1, H2),
        "w3": a["W_top3"].reshape(1, H2),
    }
    for f in range(FEATURES):
        arrays[f"tbl_{f}"] = a[f"tbl_{f}"]
    nc = bacc.Bacc("TRN2", target_bir_lowering=False, num_devices=1)
    aps = {name: nc.dram_tensor(name, x.shape, mybir.dt.from_np(x.dtype), kind="ExternalInput").ap()
           for name, x in arrays.items()}
    out = nc.dram_tensor("out", (B, 1), mybir.dt.float32, kind="ExternalOutput").ap()
    dlrm_kernel(nc, aps["ids"], aps["hot_ids"], aps["dense_t"], [aps[f"tbl_{f}"] for f in range(FEATURES)],
                aps["w_pairs"], aps["w_dense"], aps["w2"], aps["b2"], aps["w3"], out)
    r = run_bass_kernel_spmd(nc, [arrays], core_ids=[0])
    return r.results[0]["out"]
```

```python
import concourse.bass as bass
from concourse import mybir
from contextlib import ExitStack

B, D, P = 512, 128, 128
TILES = B // P
FEATURES = 26
DENSE = FEATURES
SLOTS = FEATURES + 1
PAIRS = SLOTS * (SLOTS - 1) // 2
H1, H2 = 512, 256
ROWS = [125000, 1000, 1250, 1250, 1250, 1250, 12500, 1000, 12500, 12500, 12500, 12500, 1000,
        1250, 1250, 12500, 12500, 1000, 1000, 12500, 1250, 1250, 1000, 1000, 1250, 1250]
ONE_HOT = [1, 7, 12, 17, 18, 22, 23]
GATHERED = [f for f in range(FEATURES) if f not in ONE_HOT]
ORDER = GATHERED + ONE_HOT + [DENSE]
N_HOT, N_GATHERED = len(ONE_HOT), len(GATHERED)
ROW_PARTS = 125
CHUNKS = [ROWS[f] // ROW_PARTS for f in ONE_HOT]
MAX_CHUNKS = max(CHUNKS)
QUAD = 32
QUADS = P // QUAD
COLS = SLOTS - 1
QCOLS = -(-COLS // QUADS)
BANK = 512
GROUP = 4
BANK_GROUPS = 4
SPAN_BANKS = 2
SPAN_ROWS = BANK_GROUPS * SPAN_BANKS
SPANS = QUAD // SPAN_ROWS
HOT_RING, TABLE_RING, IDB_RING, GATHER_RING = 8, 2, 3, 2
PAIR_PARTS = [(0, 3), (3, QCOLS)]
PARTS = len(PAIR_PARTS)
W_CHUNKS = QCOLS + 1

W_ORDER = [QCOLS, *range(QCOLS)]
assert SPANS * 2 == W_CHUNKS


def quad_cols(q):
    return min(QCOLS, COLS - q * QCOLS)


def plan():
    transposes = [("transpose", t, s) for t in range(TILES) for s in range(0, N_GATHERED, GROUP)]
    steps = []

    def take(n=0, upto=-1):
        while transposes and (n > 0 or transposes[0][1] <= upto):
            steps.append(transposes.pop(0))
            n -= 1

    for i in range(N_HOT):
        steps.append(("hot", i))
        take(1 if i >= 1 else 0)
    for t in range(TILES):
        take(upto=t)
        done = {0: [("turn", t - 2)], 1: [("layer2", t - 2)]} if t >= 2 else {}
        for m in range(SPANS):
            steps.append(("dots", t, m))
            steps += done.get(m, [])
            if t == 1:
                steps += [("weights", c) for c in W_ORDER[2 * m:2 * m + 2]]
        steps.append(("split", t))
        take(2)
        if t >= 1:
            steps.append(("layer1", t - 1))
    t = TILES - 1
    return steps + [("layer1", t), ("turn", t - 1), ("turn", t), ("layer2", t - 1), ("layer2", t)]


def dlrm_kernel(nc, ids, hot_ids, dense_t, tables, w_pairs, w_dense, w2, b2, w3, out):
    f32, f32r, i32 = mybir.dt.float32, mybir.dt.float32r, mybir.dt.int32
    ALU, ACT = mybir.AluOpType, mybir.ActivationFunctionType
    STEPS = plan()

    with ExitStack() as ctx:
        def sb(name, shape, dt=f32):
            return ctx.enter_context(nc.sbuf_tensor(name, shape, dt))

        def pb(name, banks=1):
            return ctx.enter_context(nc.psum_tensor(name, [P, banks * BANK], f32))

        def sem(name):
            return ctx.enter_context(nc.semaphore(name))

        idx = sb("idx", [P, TILES * FEATURES], i32)
        n_raw = TABLE_RING * MAX_CHUNKS * D
        arrivals = sb("arrivals", [P, max(n_raw + IDB_RING * B, W_CHUNKS * H1)])
        table_raw = arrivals[0:ROW_PARTS, 0:n_raw].rearrange("p (r n) -> p r n", r=TABLE_RING)
        hot_ids_b = arrivals[0:ROW_PARTS, n_raw:n_raw + IDB_RING * B].bitcast(i32).rearrange(
            "p (r b) -> p r b", r=IDB_RING)
        w1_raw = arrivals[:, 0:W_CHUNKS * H1].rearrange("p (c n) -> p c n", c=W_CHUNKS)
        row_numbers = {c: sb(f"row_numbers{c}", [ROW_PARTS, c]) for c in sorted(set(CHUNKS))}
        table_hi = sb("table_hi", [ROW_PARTS, TABLE_RING, MAX_CHUNKS * D], f32r)
        table_lo = sb("table_lo", [ROW_PARTS, TABLE_RING, MAX_CHUNKS * D], f32r)
        one_hot = sb("one_hot", [ROW_PARTS, HOT_RING, B], f32r)
        gathered = sb("gathered", [P, GATHER_RING, N_GATHERED, D])
        combined_t = sb("combined_t", [P, TILES, QUAD, QUADS, QUAD])
        x_t = sb("x_t", [P, B])
        x_hi = sb("x_hi", [P, B], f32r)
        x_lo = sb("x_lo", [P, B], f32r)
        pairs = sb("pairs", [P, QCOLS, P])
        pairs_hi = sb("pairs_hi", [P, 2, QCOLS, P], f32r)
        pairs_lo = sb("pairs_lo", [P, 2, QCOLS, P], f32r)
        w1_hi = sb("w1_hi", [P, W_CHUNKS, H1], f32r)
        w1_lo = sb("w1_lo", [P, W_CHUNKS, H1], f32r)
        w2_sb = sb("w2_sb", [P, H1 // P, H2])
        b2_b = sb("b2_b", [P, H2])
        w3_b = sb("w3_b", [P, H2])
        h1 = sb("h1", [P, 2, H1])
        h1_t = sb("h1_t", [P, 2, H1])
        h2 = sb("h2", [P, H2])
        h2_w3 = sb("h2_w3", [P, H2])
        y = sb("y", [P, TILES])
        ident = sb("ident", [P, P])

        slot_banks = [pb(f"slot_bank{i}") for i in range(2)]
        dot_spans = [pb(f"dot_span{i}", SPAN_BANKS) for i in range(2)]
        h_bank, ht_bank = pb("h_bank"), pb("ht_bank")
        h_banks = [h_bank] * (TILES - 1) + [slot_banks[0]]
        ht_banks = [ht_bank] * (TILES - 1) + [slot_banks[1]]

        ids_in, x_in, w2_in, b2_in, w3_in = (sem(n) for n in ("ids_in", "x_in", "w2_in", "b2_in", "w3_in"))
        hot_ids_in = [sem(f"hot_ids_in{i}") for i in range(IDB_RING)]
        table_in = [sem(f"table_in{i}") for i in range(TABLE_RING)]
        w1_in = [sem(f"w1_in{c}") for c in range(W_CHUNKS)]
        n_banks = -(-N_GATHERED // GROUP)
        rows_in = [[sem(f"rows_in{r}_{g}") for g in range(n_banks)] for r in range(GATHER_RING)]
        y_out = sem("y_out")
        ident_zero, ident_done, rows_numbered = sem("ident_zero"), sem("ident_done"), sem("rows_numbered")
        pads_done = sem("pads_done")
        table_hi_done, table_lo_done = sem("table_hi_done"), sem("table_lo_done")
        hot_built, hot_used = sem("hot_built"), sem("hot_used")
        transposed, slot_bank_free = sem("transposed"), sem("slot_bank_free")
        x_hi_done, x_lo_done, x_slot_done = sem("x_hi_done"), sem("x_lo_done"), sem("x_slot_done")
        w1_hi_done, w1_lo_done = sem("w1_hi_done"), sem("w1_lo_done")
        dot_span_full = sem("dot_span_full")
        moved_dve, moved_act = sem("moved_dve"), sem("moved_act")
        pairs_hi_done, pairs_lo_done = sem("pairs_hi_done"), sem("pairs_lo_done")
        h1_full, h1_done, h1t_full, h1t_done = sem("h1_full"), sem("h1_done"), sem("h1t_full"), sem("h1t_done")
        h2_full, h2_done, h2_relu, y_done = sem("h2_full"), sem("h2_done"), sem("h2_relu"), sem("y_done")

        block = ctx.enter_context(nc.Block())

        def hot_slot(i):
            return combined_t[:, :, :, :, i].rearrange("p t k j -> p t j k")

        def by_batch(ap):
            return ap.rearrange("p (t j k) -> p t j k", t=TILES, j=QUADS)

        bank_no, banks_before, k = {}, {}, 0
        for step in STEPS:
            if step[0] in ("hot", "transpose"):
                bank_no[step] = k
                k += 1
            else:
                banks_before[step] = k
        hot_before = [sum(CHUNKS[:i]) for i in range(N_HOT + 1)]

        def move_dots(copy, t, m, quads):
            span = dot_spans[(t * SPANS + m) % 2][:].rearrange("p (b n) -> p b n", b=SPAN_BANKS)
            for j in quads:
                for q in range(QUADS):
                    n = quad_cols(q)
                    at = q * QCOLS + j * COLS
                    src = span[j * QUAD:j * QUAD + SLOTS, :, 0:BANK_GROUPS * QUADS * COLS].rearrange(
                        "p b (k c) -> p b k c", k=BANK_GROUPS)[:, :, :, at:at + n]
                    k = j * QUAD + m * SPAN_ROWS
                    dst = pairs[q * QUAD:q * QUAD + SLOTS, 0:n, k:k + SPAN_ROWS].rearrange(
                        "p c (b k) -> p b k c", b=SPAN_BANKS)
                    last = copy(dst, src)
            return last

        @block.sync
        def _(sp):
            sp.dma_start(idx[:], ids).then_inc(ids_in, 16)

            def load_hot(i):
                if i >= IDB_RING:
                    sp.wait_ge(hot_built, hot_before[i - IDB_RING + 1])
                sp.dma_start(hot_ids_b[:, i % IDB_RING, :],
                             hot_ids[i:i + 1, :].partition_broadcast(ROW_PARTS).rearrange("p o b -> p (o b)")
                             ).then_inc(hot_ids_in[i % IDB_RING], 16)
                if i >= TABLE_RING:
                    sp.wait_ge(table_lo_done, i - TABLE_RING + 1)
                n = CHUNKS[i] * D
                src = tables[ONE_HOT[i]].rearrange("(p c) d -> p (c d)", p=ROW_PARTS)
                for lo, hi in ((0, 112), (112, ROW_PARTS)):
                    sp.dma_start(table_raw[lo:hi, i % TABLE_RING, 0:n], src[lo:hi, :]
                                 ).then_inc(table_in[i % TABLE_RING], 16)

            for i in range(TABLE_RING):
                load_hot(i)
            sp.dma_start(x_t[:], dense_t).then_inc(x_in, 16)
            for i in range(TABLE_RING, N_HOT):
                load_hot(i)
            sp.wait_ge(table_lo_done, N_HOT)
            sp.wait_ge(hot_built, hot_before[N_HOT])
            for c in W_ORDER:
                src = w_pairs[:, c * H1:(c + 1) * H1] if c < QCOLS else w_dense
                sp.dma_start(w1_raw[:, c, :], src).then_inc(w1_in[c], 16)
            sp.dma_start(w2_sb[:], w2.rearrange("(c p) n -> p c n", p=P)).then_inc(w2_in, 16)
            sp.dma_start(b2_b[:], b2.partition_broadcast(P).rearrange("p o n -> p (o n)")).then_inc(b2_in, 16)
            sp.dma_start(w3_b[:], w3.partition_broadcast(P).rearrange("p o n -> p (o n)")).then_inc(w3_in, 16)

            for t in range(TILES - 1):
                sp.wait_ge(y_done, t + 1)
                sp.dma_start(out[t * P:(t + 1) * P, :], y[:, t:t + 1]).then_inc(y_out, 16)
            sp.wait_ge(y_done, TILES)
            sp.dma_start(out[(TILES - 1) * P:B, :], y[:, TILES - 1:TILES]).then_inc(y_out, 16)
            sp.wait_ge(y_out, 16 * TILES)

        @block.gpsimd
        def _(pool):
            for c in row_numbers:
                pool.iota(row_numbers[c][:], pattern=[[1, c]], base=0, channel_multiplier=c,
                          allow_small_or_imprecise_dtypes=True).then_inc(rows_numbered, 1)
            pool.memset(ident[:], 0.0).then_inc(ident_zero, 1)
            pool.wait_ge(ident_zero, 1)
            pool.affine_select(out=ident[:], in_=ident[:], compare_op=ALU.not_equal, fill=1.0,
                               base=0, pattern=[[-1, P]], channel_multiplier=1).then_inc(ident_done, 1)
            pool.wait_ge(ids_in, 16)
            for t in range(TILES):
                for n, f in enumerate(GATHERED):
                    if t >= GATHER_RING and n % GROUP == 0:
                        pool.wait_ge(transposed, (t - GATHER_RING) * n_banks + n // GROUP + 1)
                    pool.indirect_dma_start(
                        gathered[:, t % GATHER_RING, n, :], None, tables[f],
                        bass.IndirectOffsetOnAxis(ap=idx[:, t * FEATURES + f:t * FEATURES + f + 1], axis=0)
                    ).then_inc(rows_in[t % GATHER_RING][n // GROUP], 16)

        @block.scalar
        def _(act):
            def split_table(i):
                act.wait_ge(table_in[i % TABLE_RING], 32 * (i // TABLE_RING + 1))
                if i >= TABLE_RING:
                    act.wait_ge(hot_used, hot_before[i - TABLE_RING + 1])
                n = CHUNKS[i] * D
                act.activation(table_hi[:, i % TABLE_RING, 0:n], table_raw[:, i % TABLE_RING, 0:n],
                               ACT.Copy).then_inc(table_hi_done, 1)

            for i in range(TABLE_RING):
                split_table(i)
            act.wait_ge(x_in, 16)
            act.activation(x_hi[:], x_t[:], ACT.Copy).then_inc(x_hi_done, 1)
            act.activation(hot_slot(SLOTS - 1), by_batch(x_t[:]),
                           ACT.Copy).then_inc(x_slot_done, 1)

            for step in STEPS:
                kind, i = step[0], step[1]
                if kind == "hot":
                    n = bank_no[step]
                    act.wait_ge(hot_used, hot_before[i + 1])
                    act.activation(hot_slot(N_GATHERED + i),
                                   by_batch(slot_banks[n % 2][:]),
                                   ACT.Copy).then_inc(slot_bank_free, 1)
                    if i + TABLE_RING < N_HOT:
                        split_table(i + TABLE_RING)
                elif kind == "transpose":
                    n, s = bank_no[step], step[2]
                    g = min(GROUP, N_GATHERED - s)
                    act.wait_ge(transposed, i * n_banks + s // GROUP + 1)
                    act.activation(combined_t[:, i, :, :, s:s + g].rearrange("p k j g -> p g j k"),
                                   slot_banks[n % 2][:, 0:g * P].rearrange("p (g j k) -> p g j k", g=g, j=QUADS),
                                   ACT.Copy).then_inc(slot_bank_free, 1)
                elif kind == "dots":
                    m = step[2]
                    act.wait_ge(dot_span_full, i * SPANS + m + 1)
                    if m == 0 and i == 0:
                        act.wait_ge(pads_done, 3)
                    elif m == 0:
                        act.wait_ge(pairs_lo_done, PARTS * i)
                    move_dots(lambda d, a: act.activation(d, a, ACT.Copy), i, m, (2, 3)).then_inc(moved_act, 1)
                elif kind == "split":
                    act.wait_ge(moved_act, SPANS * (i + 1))
                    act.wait_ge(moved_dve, SPANS * (i + 1))
                    if i >= 2:
                        act.wait_ge(h1_full, i - 1)
                    for lo, hi in PAIR_PARTS:
                        act.activation(pairs_hi[:, i % 2, lo:hi, :], pairs[:, lo:hi, :],
                                       ACT.Copy).then_inc(pairs_hi_done, 1)
                elif kind == "weights":
                    act.wait_ge(w1_in[i], 16)
                    act.activation(w1_hi[:, i, :], w1_raw[:, i, :], ACT.Copy).then_inc(w1_hi_done, 1)
                elif kind == "layer1":
                    act.wait_ge(h1_full, i + 1)
                    if i >= 2:
                        act.wait_ge(h1t_full, i - 1)
                    act.activation(h1[:, i % 2, :], h_banks[i][:], ACT.Relu).then_inc(h1_done, 1)

        @block.vector
        def _(dve):
            dve.memset(combined_t[:, :, :, :, SLOTS:QUAD], 0.0).then_inc(pads_done, 1)
            dve.memset(pairs[:, 0, :], 1.0).then_inc(pads_done, 1)
            dve.memset(pairs[:, 1:QCOLS, :], 0.0).then_inc(pads_done, 1)

            def split_table(i):
                dve.wait_ge(table_hi_done, i + 1)
                if i >= TABLE_RING:
                    dve.wait_ge(hot_used, hot_before[i - TABLE_RING + 1])
                n = CHUNKS[i] * D
                dve.tensor_tensor(table_lo[:, i % TABLE_RING, 0:n], table_raw[:, i % TABLE_RING, 0:n],
                                  table_hi[:, i % TABLE_RING, 0:n].bitcast(f32),
                                  ALU.subtract).then_inc(table_lo_done, 1)

            dve.wait_ge(rows_numbered, len(row_numbers))
            for step in STEPS:
                kind, i = step[0], step[1]
                if kind == "hot":
                    dve.wait_ge(hot_ids_in[i % IDB_RING], 16 * (i // IDB_RING + 1))
                    for c in range(CHUNKS[i]):
                        n = hot_before[i] + c
                        if n == 1:
                            split_table(0)
                        if n >= HOT_RING:
                            dve.wait_ge(hot_used, n - HOT_RING + 1)
                        dve.tensor_scalar(one_hot[:, n % HOT_RING, :], hot_ids_b[:, i % IDB_RING, :],
                                          row_numbers[CHUNKS[i]][:, c:c + 1], None,
                                          ALU.is_equal).then_inc(hot_built, 1)
                    if i + 1 < N_HOT:
                        split_table(i + 1)
                    if i == 1:
                        dve.wait_ge(x_hi_done, 1)
                        dve.tensor_tensor(x_lo[:], x_t[:], x_hi[:].bitcast(f32), ALU.subtract).then_inc(x_lo_done, 1)
                elif kind == "dots":
                    m = step[2]
                    dve.wait_ge(dot_span_full, i * SPANS + m + 1)
                    if m == 0 and i >= 1:
                        dve.wait_ge(pairs_lo_done, PARTS * i)
                    move_dots(dve.tensor_copy, i, m, (0, 1)).then_inc(moved_dve, 1)
                elif kind == "split":
                    for n, (lo, hi) in enumerate(PAIR_PARTS):
                        dve.wait_ge(pairs_hi_done, PARTS * i + n + 1)
                        dve.tensor_tensor(pairs_lo[:, i % 2, lo:hi, :], pairs[:, lo:hi, :],
                                          pairs_hi[:, i % 2, lo:hi, :].bitcast(f32),
                                          ALU.subtract).then_inc(pairs_lo_done, 1)
                elif kind == "weights":
                    dve.wait_ge(w1_hi_done, W_ORDER.index(i) + 1)
                    dve.tensor_tensor(w1_lo[:, i, :], w1_raw[:, i, :], w1_hi[:, i, :].bitcast(f32),
                                      ALU.subtract).then_inc(w1_lo_done, 1)
                elif kind == "turn":
                    dve.wait_ge(h1t_full, i + 1)
                    if i >= 2:
                        dve.wait_ge(h2_full, i - 1)
                    dve.tensor_copy(h1_t[:, i % 2, :], ht_banks[i][:]).then_inc(h1t_done, 1)
                elif kind == "layer2":
                    if i == 0:
                        dve.wait_ge(b2_in, 16)
                        dve.wait_ge(w3_in, 16)
                    dve.wait_ge(h2_full, i + 1)
                    if i >= 1:
                        dve.wait_ge(y_done, i)
                    dve.tensor_tensor(h2[:], h_banks[i][:, 0:H2], b2_b[:], ALU.add).then_inc(h2_done, 1)
                    dve.wait_ge(h2_done, i + 1)
                    dve.scalar_tensor_tensor(out=h2_w3[:], in0=h2[:], scalar=0.0, in1=w3_b[:], op0=ALU.max,
                                             op1=ALU.mult, accum_out=y[:, i:i + 1]).then_inc(y_done, 1)

        @block.tensor
        def _(pe):
            pe.wait_ge(ident_done, 1)
            for step in STEPS:
                kind, i = step[0], step[1]
                if kind in ("hot", "transpose"):
                    n = bank_no[step]
                    bank = slot_banks[n % 2]
                    if n >= 2:
                        pe.wait_ge(slot_bank_free, n - 1)
                if kind == "hot":
                    pe.wait_ge(table_lo_done, i + 1)
                    r = i % TABLE_RING
                    for c in range(CHUNKS[i]):
                        m = hot_before[i] + c
                        pe.wait_ge(hot_built, m + 1)
                        pe.matmul(bank[:], table_hi[:, r, c * D:(c + 1) * D], one_hot[:, m % HOT_RING, :],
                                  start=(c == 0), stop=False)
                        last = pe.matmul(bank[:], table_lo[:, r, c * D:(c + 1) * D], one_hot[:, m % HOT_RING, :],
                                         start=False, stop=(c == CHUNKS[i] - 1))
                        last.then_inc(hot_used, 1)
                elif kind == "transpose":
                    s = step[2]
                    g = min(GROUP, N_GATHERED - s)
                    pe.wait_ge(rows_in[i % GATHER_RING][s // GROUP], 16 * g * (i // GATHER_RING + 1))
                    for m in range(g):
                        last = pe.transpose(bank[:, m * P:(m + 1) * P], gathered[:, i % GATHER_RING, s + m, :], ident[:])
                    last.then_inc(transposed, 1)
                elif kind == "dots":
                    m = step[2]
                    n = i * SPANS + m
                    if m == 0:
                        pe.wait_ge(slot_bank_free, banks_before[step])
                    if n == 0:
                        pe.wait_ge(x_slot_done, 1)
                        pe.wait_ge(pads_done, 1)
                    if n >= 2:
                        pe.wait_ge(moved_dve, n - 1)
                        pe.wait_ge(moved_act, n - 1)
                    for g in range(SPAN_ROWS):
                        k = m * SPAN_ROWS + g
                        at = g // BANK_GROUPS * BANK + g % BANK_GROUPS * QUADS * COLS
                        last = pe.matmul(dot_spans[n % 2][:, at:at + QUADS * COLS],
                                         combined_t[:, i, k].rearrange("p j s -> p (j s)"),
                                         combined_t[:, i, k, :, 1:SLOTS],
                                         start=True, stop=True)
                    last.then_inc(dot_span_full, 1)
                elif kind == "layer1":
                    if i == 0:
                        pe.wait_ge(x_lo_done, 1)
                    elif i == TILES - 1:
                        pe.wait_ge(slot_bank_free, banks_before[step])
                    else:
                        pe.wait_ge(h2_done, i)
                    r = i % 2
                    parts = [(x_hi[:, i * P:(i + 1) * P], x_lo[:, i * P:(i + 1) * P], QCOLS)]
                    parts += [(pairs_hi[:, r, c, :], pairs_lo[:, r, c, :], c) for c in range(QCOLS)]
                    for n, (hi, lo, c) in enumerate(parts):
                        for m, (first, _) in enumerate(PAIR_PARTS):
                            if c == first:
                                pe.wait_ge(pairs_lo_done, PARTS * i + m + 1)
                        if i == 0:
                            pe.wait_ge(w1_lo_done, n + 1)
                        pe.matmul(h_banks[i][:], hi, w1_hi[:, c, :], start=(n == 0), stop=False)
                        pe.matmul(h_banks[i][:], hi, w1_lo[:, c, :], start=False, stop=False)
                        last = pe.matmul(h_banks[i][:], lo, w1_hi[:, c, :], start=False, stop=(n == len(parts) - 1))
                    last.then_inc(h1_full, 1)
                elif kind == "turn":
                    pe.wait_ge(h1_done, i + 1)
                    if 1 <= i < TILES - 1:
                        pe.wait_ge(h1t_done, i)
                    for c in range(H1 // P):
                        last = pe.transpose(ht_banks[i][:, c * P:(c + 1) * P], h1[:, i % 2, c * P:(c + 1) * P], ident[:])
                    last.then_inc(h1t_full, 1)
                elif kind == "layer2":
                    if i == 0:
                        pe.wait_ge(w2_in, 16)
                    pe.wait_ge(h1t_done, i + 1)
                    for c in range(H1 // P):
                        last = pe.matmul(h_banks[i][:, 0:H2], h1_t[:, i % 2, c * P:(c + 1) * P], w2_sb[:, c, :],
                                         start=(c == 0), stop=(c == H1 // P - 1))
                    last.then_inc(h2_full, 1)


def pair_row(f, g):
    f, g = min(f, g), max(f, g)
    return f * SLOTS - f * (f + 1) // 2 + g - f - 1


def kernel(**inputs):
    import numpy as np
    import concourse.bacc as bacc
    from concourse.bass_utils import run_bass_kernel_spmd

    a = {name: np.ascontiguousarray(x) for name, x in inputs.items()}
    w_pairs = np.zeros((P, QCOLS, H1), a["W_top1"].dtype)
    for g in range(1, SLOTS):
        q, c = divmod(g - 1, QCOLS)
        for f in range(g):
            w_pairs[q * QUAD + f, c] = a["W_top1"][pair_row(ORDER[f], ORDER[g])]
    w_pairs[SLOTS, 0] = a["b_top1"]
    arrays = {
        "ids": np.ascontiguousarray(a["ids"].reshape(TILES, P, FEATURES).transpose(1, 0, 2).reshape(P, -1)),
        "hot_ids": np.ascontiguousarray(a["ids"].T[ONE_HOT]),
        "dense_t": np.ascontiguousarray(a["r_dense_x"].T),
        "w_pairs": w_pairs.reshape(P, -1),
        "w_dense": np.ascontiguousarray(a["W_top1"][PAIRS:]),
        "w2": a["W_top2"],
        "b2": a["b_top2"].reshape(1, H2),
        "w3": a["W_top3"].reshape(1, H2),
    }
    for f in range(FEATURES):
        arrays[f"tbl_{f}"] = a[f"tbl_{f}"]
    nc = bacc.Bacc("TRN2", target_bir_lowering=False, num_devices=1)
    aps = {name: nc.dram_tensor(name, x.shape, mybir.dt.from_np(x.dtype), kind="ExternalInput").ap()
           for name, x in arrays.items()}
    out = nc.dram_tensor("out", (B, 1), mybir.dt.float32, kind="ExternalOutput").ap()
    dlrm_kernel(nc, aps["ids"], aps["hot_ids"], aps["dense_t"], [aps[f"tbl_{f}"] for f in range(FEATURES)],
                aps["w_pairs"], aps["w_dense"], aps["w2"], aps["b2"], aps["w3"], out)
    r = run_bass_kernel_spmd(nc, [arrays], core_ids=[0])
    return r.results[0]["out"]
```

```python
import concourse.bass as bass
from concourse import mybir
from contextlib import ExitStack

B, D, P = 512, 128, 128
TILES = B // P
FEATURES = 26
DENSE = FEATURES
SLOTS = FEATURES + 1
PAIRS = SLOTS * (SLOTS - 1) // 2
H1, H2 = 512, 256
HALF = H1 // 2
ROWS = [125000, 1000, 1250, 1250, 1250, 1250, 12500, 1000, 12500, 12500, 12500, 12500, 1000,
        1250, 1250, 12500, 12500, 1000, 1000, 12500, 1250, 1250, 1000, 1000, 1250, 1250]
ONE_HOT = [1, 7, 12, 17, 18, 22, 23]
GATHERED = [f for f in range(FEATURES) if f not in ONE_HOT]
ORDER = GATHERED + ONE_HOT + [DENSE]
N_HOT, N_GATHERED = len(ONE_HOT), len(GATHERED)
ROW_PARTS = 125
CHUNKS = [ROWS[f] // ROW_PARTS for f in ONE_HOT]
MAX_CHUNKS = max(CHUNKS)
QUAD = 32
QUADS = P // QUAD
COLS = SLOTS - 1
QCOLS = -(-COLS // QUADS)
BANK = 512
GROUPS = [(0, 4), (4, 8), (8, 12), (12, 16), (16, 18), (18, N_GATHERED)]
BANK_GROUPS = 4
SPAN_BANKS = 2
SPAN_ROWS = BANK_GROUPS * SPAN_BANKS
SPANS = QUAD // SPAN_ROWS
HOT_RING, TABLE_RING, IDB_RING, GATHER_RING = 8, 2, 3, 2
FIRST_ONE_HOTS = 4
WARM_UP = 25
PAIR_PARTS = [(0, 1), (1, 3), (3, QCOLS)]
PARTS = len(PAIR_PARTS)
W_CHUNKS = QCOLS + 1
W_PLACES = [2, 3, 5, 6, 0, 1, 4, 7]
W_ORDER = [QCOLS, *range(QCOLS)]
L1_PARTS = [(0, 1), (1, 4), (4, 6), (6, W_CHUNKS)]
W_EARLY = 4


def quad_cols(q):
    return min(QCOLS, COLS - q * QCOLS)


def plan():
    transposes = [("transpose", t, g) for t in range(TILES) for g in range(len(GROUPS))]
    steps = []

    def take(n):
        for _ in range(n):
            steps.append(transposes.pop(0))
            if steps[-1][1] < TILES - 1 and steps[-1][2] == len(GROUPS) - 2:
                steps.append(transposes.pop(0))

    def weights(c):
        return [("weights_hi", c), ("weights_lo", c)]

    def dots(t, beside):
        for m in range(SPANS):
            steps.append(("dots", t, m))
            for step in beside[m]:
                take(1) if step == "take" else steps.append(step)
        steps.append(("split", t))

    for i in range(N_HOT):
        steps.append(("hot", i))
        if i in (2, 3):
            steps.append(("x_hi" if i == 2 else "x_slot", 0))
        if i >= N_HOT - 2:
            n = (i - N_HOT + 2) * W_EARLY // 2
            steps.extend(("weights_hi", c) for c in W_ORDER[n:n + W_EARLY // 2])
        steps.append(("hot_slot", i))
        take(1 if i >= 1 else 0)
    take(1)
    steps.extend([("pads", 0), ("x_lo", 0)])
    steps.extend(("weights_lo", c) for c in W_ORDER[:W_EARLY])
    dots(0, [weights(3), ["take"] + weights(4), weights(5), []])
    take(1)
    steps.append(("layer1", 0, 0))
    steps.extend(weights(6))
    steps.append(("layer1", 0, 1))
    take(1)
    steps.extend([("layer1", 0, 2), ("layer1", 0, 3)])
    dots(1, [[("turn", 0)], [], ["take"], []])
    steps.append(("layer2", 0))
    take(1)
    steps.extend([("layer1", 1, 0), ("layer1", 1, 1)])
    take(1)
    steps.append(("layer1", 1, 2))
    take(2)
    steps.append(("layer1", 1, 3))
    dots(2, [[("turn", 1)], [], ["take"], []])
    steps.append(("layer2", 1))
    take(1)
    steps.extend([("layer1", 2, 0), ("layer1", 2, 1)])
    take(1)
    steps.append(("layer1", 2, 2))
    take(1)
    steps.append(("layer1", 2, 3))
    take(2)
    steps.append(("turn", 2))
    dots(3, [[]] * SPANS)
    return steps + [("layer2", 2), ("last_layer1", 0), ("last_layer1", 1), ("last_turn", 0), ("last_bias", 0),
                    ("last_turn", 1), ("last_layer2", 0), ("last_layer2", 1)]


def dlrm_kernel(nc, ids, hot_ids, dense_t, tables, w_pairs, w_dense, w2, b2, w3, out):
    f32, f32r, i32 = mybir.dt.float32, mybir.dt.float32r, mybir.dt.int32
    ALU, ACT = mybir.AluOpType, mybir.ActivationFunctionType
    STEPS = plan()

    with ExitStack() as ctx:
        def sb(name, shape, dt=f32):
            return ctx.enter_context(nc.sbuf_tensor(name, shape, dt))

        def pb(name, banks=1):
            return ctx.enter_context(nc.psum_tensor(name, [P, banks * BANK], f32))

        def sem(name):
            return ctx.enter_context(nc.semaphore(name))

        idx = sb("idx", [P, TILES * FEATURES], i32)
        n_raw = TABLE_RING * MAX_CHUNKS * D
        arrivals = sb("arrivals", [P, max(n_raw + IDB_RING * B, W_CHUNKS * H1)])
        table_raw = arrivals[0:ROW_PARTS, 0:n_raw].rearrange("p (r n) -> p r n", r=TABLE_RING)
        hot_ids_b = arrivals[0:ROW_PARTS, n_raw:n_raw + IDB_RING * B].bitcast(i32).rearrange(
            "p (r b) -> p r b", r=IDB_RING)
        w1_raw = arrivals[:, 0:W_CHUNKS * H1].rearrange("p (c n) -> p c n", c=W_CHUNKS)
        row_numbers = {c: sb(f"row_numbers{c}", [ROW_PARTS, c]) for c in sorted(set(CHUNKS))}
        last_rows = sb("last_rows", [ROW_PARTS, len(row_numbers)])
        table_hi = sb("table_hi", [ROW_PARTS, TABLE_RING, MAX_CHUNKS * D], f32r)
        table_lo = sb("table_lo", [ROW_PARTS, TABLE_RING, MAX_CHUNKS * D], f32r)
        one_hot = sb("one_hot", [ROW_PARTS, HOT_RING, B], f32r)
        distance = sb("distance", [ROW_PARTS, B])
        gathered = sb("gathered", [P, GATHER_RING, N_GATHERED, D])
        combined_t = sb("combined_t", [P, TILES, QUAD, QUADS, QUAD])
        x_t = sb("x_t", [P, B])
        x_hi = sb("x_hi", [P, B], f32r)
        x_lo = sb("x_lo", [P, B], f32r)
        pairs = sb("pairs", [P, QCOLS, P])
        pairs_hi = sb("pairs_hi", [P, 2, QCOLS, P], f32r)
        pairs_lo = sb("pairs_lo", [P, 2, QCOLS, P], f32r)
        w1_hi = sb("w1_hi", [P, W_CHUNKS, H1], f32r)
        w1_lo = sb("w1_lo", [P, W_CHUNKS, H1], f32r)
        w2_sb = sb("w2_sb", [P, H1 // P, H2])
        b2_b = sb("b2_b", [P, H2])
        w3_b = sb("w3_b", [P, H2])
        h1 = sb("h1", [P, 2, H1])
        h1_t = sb("h1_t", [P, 2, H1])
        h2 = sb("h2", [P, H2])
        h2_w3 = sb("h2_w3", [P, H2])
        y = sb("y", [P, TILES])
        ident = sb("ident", [P, P])
        one = sb("one", [1, P])

        slot_banks = [pb(f"slot_bank{i}") for i in range(2)]
        dot_spans = [pb(f"dot_span{i}", SPAN_BANKS) for i in range(2)]
        h_bank, ht_bank = pb("h_bank"), pb("ht_bank")
        hot_banks = [h_bank, ht_bank]
        h_halves = [h_bank, slot_banks[0]]
        ht_halves = [slot_banks[1], dot_spans[0]]

        ids_in, x_in, w2_in, b2_in, w3_in = (sem(n) for n in ("ids_in", "x_in", "w2_in", "b2_in", "w3_in"))
        hot_ids_in = [sem(f"hot_ids_in{i}") for i in range(IDB_RING)]
        table_in = [sem(f"table_in{i}") for i in range(TABLE_RING)]
        w1_in = [sem(f"w1_in{c}") for c in range(W_CHUNKS)]
        n_groups = len(GROUPS)
        rows_in = [[sem(f"rows_in{r}_{g}") for g in range(n_groups)] for r in range(GATHER_RING)]
        y_out = sem("y_out")
        ident_zero, ident_done, rows_numbered = sem("ident_zero"), sem("ident_done"), sem("rows_numbered")
        pads_done = sem("pads_done")
        table_hi_done, table_lo_done = sem("table_hi_done"), sem("table_lo_done")
        hot_built, last_hot_built, hot_used = sem("hot_built"), sem("last_hot_built"), sem("hot_used")
        last_rows_done = sem("last_rows_done")
        distance_done = sem("distance_done")
        transposed, slots_filled = sem("transposed"), sem("slots_filled")
        hot_slot_filled = sem("hot_slot_filled")
        x_hi_done, x_lo_done, x_slot_done = sem("x_hi_done"), sem("x_lo_done"), sem("x_slot_done")
        w1_hi_done, w1_lo_done = sem("w1_hi_done"), sem("w1_lo_done")
        dot_span_full = sem("dot_span_full")
        moved_dve, moved_act = sem("moved_dve"), sem("moved_act")
        pairs_hi_done, pairs_lo_done = sem("pairs_hi_done"), sem("pairs_lo_done")
        h1_full, h1_done, h1t_full, h1t_done = sem("h1_full"), sem("h1_done"), sem("h1t_full"), sem("h1t_done")
        h2_full, h2_done, y_done = sem("h2_full"), sem("h2_done"), sem("y_done")
        one_done = sem("one_done")

        block = ctx.enter_context(nc.Block())

        def hot_slot(i):
            return combined_t[:, :, :, :, i].rearrange("p t k j -> p t j k")

        def by_batch(ap):
            return ap.rearrange("p (t j k) -> p t j k", t=TILES, j=QUADS)

        def group_no(t, g):
            return t * n_groups + g

        hot_before = [sum(CHUNKS[:i]) for i in range(N_HOT + 1)]

        def table_parts(i):
            half = CHUNKS[i] // 2 * D
            return [(0, half), (half, CHUNKS[i] * D)] if i == 0 else [(0, CHUNKS[i] * D)]

        def tables_split(i):
            return i + 1 if i >= 1 else 0

        def hots_built(eng, i, c):
            if c < CHUNKS[i] - 1:
                eng.wait_ge(hot_built, hot_before[i] - i + c + 1)
            else:
                eng.wait_ge(last_hot_built, i + 1)

        def move_dots(copy, t, m, quads):
            span = dot_spans[(t * SPANS + m) % 2][:].rearrange("p (b n) -> p b n", b=SPAN_BANKS)
            for j in quads:
                for q in range(QUADS):
                    n = quad_cols(q)
                    at = q * QCOLS + j * COLS
                    src = span[j * QUAD:j * QUAD + SLOTS, :, 0:BANK_GROUPS * QUADS * COLS].rearrange(
                        "p b (k c) -> p b k c", k=BANK_GROUPS)[:, :, :, at:at + n]
                    k = j * QUAD + m * SPAN_ROWS
                    dst = pairs[q * QUAD:q * QUAD + SLOTS, 0:n, k:k + SPAN_ROWS].rearrange(
                        "p c (b k) -> p b k c", b=SPAN_BANKS)
                    last = copy(dst, src)
            return last

        @block.sync
        def _(sp):
            sp.dma_start(idx[:], ids).then_inc(ids_in, 16)

            def load_hot(i):
                if i >= IDB_RING:
                    for c in (CHUNKS[i - IDB_RING] - 2, CHUNKS[i - IDB_RING] - 1):
                        hots_built(sp, i - IDB_RING, c)
                sp.dma_start(hot_ids_b[:, i % IDB_RING, :],
                             hot_ids[i:i + 1, :].partition_broadcast(ROW_PARTS).rearrange("p o b -> p (o b)")
                             ).then_inc(hot_ids_in[i % IDB_RING], 16)
                if i >= TABLE_RING:
                    sp.wait_ge(table_lo_done, tables_split(i - TABLE_RING + 1))
                n = CHUNKS[i] * D
                src = tables[ONE_HOT[i]].rearrange("(p c) d -> p (c d)", p=ROW_PARTS)
                for lo, hi in ((0, 112), (112, ROW_PARTS)):
                    sp.dma_start(table_raw[lo:hi, i % TABLE_RING, 0:n], src[lo:hi, :]
                                 ).then_inc(table_in[i % TABLE_RING], 16)

            for i in range(TABLE_RING):
                load_hot(i)
            sp.dma_start(x_t[:], dense_t).then_inc(x_in, 16)
            for i in range(TABLE_RING, N_HOT):
                load_hot(i)

            def load_weights(chunks):
                for c in chunks:
                    src = w_pairs[:, c * H1:(c + 1) * H1] if c < QCOLS else w_dense
                    sp.dma_start(w1_raw[:, W_PLACES[c], :], src).then_inc(w1_in[c], 16)

            load_weights([QCOLS])
            sp.wait_ge(table_lo_done, tables_split(N_HOT - 1))
            load_weights([0, 1])
            for i, chunks in ((N_HOT - 3, [2]), (N_HOT - 2, [3]), (N_HOT - 1, [4, 5, 6])):
                if i == N_HOT - 1:
                    sp.wait_ge(table_lo_done, tables_split(N_HOT))
                for c in (CHUNKS[i] - 2, CHUNKS[i] - 1):
                    hots_built(sp, i, c)
                load_weights(chunks)
            sp.dma_start(w2_sb[:], w2.rearrange("(c p) n -> p c n", p=P)).then_inc(w2_in, 16)
            sp.dma_start(b2_b[:], b2.partition_broadcast(P).rearrange("p o n -> p (o n)")).then_inc(b2_in, 16)
            sp.dma_start(w3_b[:], w3.partition_broadcast(P).rearrange("p o n -> p (o n)")).then_inc(w3_in, 16)

            for t in range(TILES - 1):
                sp.wait_ge(y_done, t + 1)
                sp.dma_start(out[t * P:(t + 1) * P, :], y[:, t:t + 1]).then_inc(y_out, 16)
            sp.wait_ge(y_done, TILES)
            sp.dma_start(out[(TILES - 1) * P:B, :], y[:, TILES - 1:TILES]).then_inc(y_out, 16)
            sp.wait_ge(y_out, 16 * TILES)

        @block.gpsimd
        def _(pool):
            for c in row_numbers:
                pool.iota(row_numbers[c][:], pattern=[[1, c]], base=0, channel_multiplier=c,
                          allow_small_or_imprecise_dtypes=True).then_inc(rows_numbered, 1)
            pool.memset(ident[:], 0.0).then_inc(ident_zero, 1)
            pool.wait_ge(ident_zero, 1)
            pool.affine_select(out=ident[:], in_=ident[:], compare_op=ALU.not_equal, fill=1.0,
                               base=0, pattern=[[-1, P]], channel_multiplier=1).then_inc(ident_done, 1)
            pool.wait_ge(ids_in, 16)
            for t in range(TILES):
                for g, (lo, hi) in enumerate(GROUPS):
                    if t >= GATHER_RING:
                        pool.wait_ge(transposed, group_no(t - GATHER_RING, g) + 1)
                    for n in range(lo, hi):
                        at = t * FEATURES + GATHERED[n]
                        pool.indirect_dma_start(
                            gathered[:, t % GATHER_RING, n, :], None, tables[GATHERED[n]],
                            bass.IndirectOffsetOnAxis(ap=idx[:, at:at + 1], axis=0)
                        ).then_inc(rows_in[t % GATHER_RING][g], 16)

        @block.scalar
        def _(act):
            def split_table(i):
                act.wait_ge(table_in[i % TABLE_RING], 32 * (i // TABLE_RING + 1))
                if i >= TABLE_RING:
                    act.wait_ge(hot_used, hot_before[i - TABLE_RING + 1])
                for lo, hi in table_parts(i):
                    act.activation(table_hi[:, i % TABLE_RING, lo:hi], table_raw[:, i % TABLE_RING, lo:hi],
                                   ACT.Copy).then_inc(table_hi_done, 1)

            def last_one_hot(i):
                if i == 0:
                    act.wait_ge(last_rows_done, len(row_numbers))
                else:
                    act.wait_ge(last_hot_built, i)
                m = hot_before[i + 1] - 1
                w = sorted(row_numbers).index(CHUNKS[i])
                act.wait_ge(hot_ids_in[i % IDB_RING], 16 * (i // IDB_RING + 1))
                act.activation(distance[:], hot_ids_b[:, i % IDB_RING, :], ACT.Abs,
                               bias=last_rows[:, w:w + 1]).then_inc(distance_done, 1)
                if m >= HOT_RING:
                    act.wait_ge(hot_used, m - HOT_RING + 1)
                act.wait_ge(distance_done, i + 1)
                act.activation(one_hot[:, m % HOT_RING, :], distance[:], ACT.Relu,
                               bias=1.0, scale=-1.0).then_inc(last_hot_built, 1)

            act.wait_ge(rows_numbered, len(row_numbers))
            for n, c in enumerate(row_numbers):
                act.activation(last_rows[:, n:n + 1], row_numbers[c][:, c - 1:c], ACT.Copy,
                               scale=-1.0).then_inc(last_rows_done, 1)
            last_one_hot(0)
            for i in range(TABLE_RING):
                split_table(i)

            for step in STEPS:
                kind, i = step[0], step[1]
                if kind == "hot" and i >= 1:
                    last_one_hot(i)
                elif kind == "hot_slot":
                    act.wait_ge(hot_used, hot_before[i + 1])
                    act.activation(hot_slot(N_GATHERED + i),
                                   by_batch(hot_banks[i % 2][:]),
                                   ACT.Copy).then_inc(hot_slot_filled, 1)
                    if i + TABLE_RING < N_HOT:
                        split_table(i + TABLE_RING)
                elif kind == "x_hi":
                    act.wait_ge(x_in, 16)
                    act.activation(x_hi[:], x_t[:], ACT.Copy).then_inc(x_hi_done, 1)
                elif kind == "x_slot":
                    act.activation(hot_slot(SLOTS - 1), by_batch(x_t[:]), ACT.Copy).then_inc(x_slot_done, 1)
                elif kind == "transpose":
                    lo, hi = GROUPS[step[2]]
                    n, g = group_no(i, step[2]), hi - lo
                    act.wait_ge(transposed, n + 1)
                    act.activation(combined_t[:, i, :, :, lo:hi].rearrange("p k j g -> p g j k"),
                                   slot_banks[n % 2][:, 0:g * P].rearrange("p (g j k) -> p g j k", g=g, j=QUADS),
                                   ACT.Copy).then_inc(slots_filled, 1)
                elif kind == "dots":
                    m = step[2]
                    act.wait_ge(dot_span_full, i * SPANS + m + 1)
                    if m == 0 and i == 0:
                        act.wait_ge(pads_done, 3)
                    elif m == 0:
                        act.wait_ge(pairs_lo_done, PARTS * i)
                    move_dots(lambda d, a: act.activation(d, a, ACT.Copy), i, m, (2, 3)).then_inc(moved_act, 1)
                elif kind == "split":
                    act.wait_ge(moved_act, SPANS * (i + 1))
                    act.wait_ge(moved_dve, SPANS * (i + 1))
                    if i >= 2:
                        act.wait_ge(h1_full, i - 1)
                    for lo, hi in PAIR_PARTS:
                        act.activation(pairs_hi[:, i % 2, lo:hi, :], pairs[:, lo:hi, :],
                                       ACT.Copy).then_inc(pairs_hi_done, 1)
                elif kind == "weights_hi":
                    act.wait_ge(w1_in[i], 16)
                    act.activation(w1_hi[:, i, :], w1_raw[:, W_PLACES[i], :], ACT.Copy).then_inc(w1_hi_done, 1)
                elif kind == "layer1" and step[2] == len(L1_PARTS) - 1:
                    act.wait_ge(h1_full, i + 1)
                    if i >= 2:
                        act.wait_ge(h1t_full, i - 1)
                    act.activation(h1[:, i % 2, :], h_bank[:], ACT.Relu).then_inc(h1_done, 1)
                elif kind == "last_layer1":
                    act.wait_ge(h1_full, TILES + i)
                    act.wait_ge(h1t_full, TILES - 2)
                    act.activation(h1[:, (TILES - 1) % 2, i * HALF:(i + 1) * HALF], h_halves[i][:, 0:HALF],
                                   ACT.Relu).then_inc(h1_done, 1)

        @block.vector
        def _(dve):
            dve.memset(combined_t[:, :, :, :, SLOTS:QUAD], 0.0).then_inc(pads_done, 1)

            def split_table(i):
                if i >= TABLE_RING:
                    dve.wait_ge(hot_used, hot_before[i - TABLE_RING + 1])
                for n, (lo, hi) in enumerate(table_parts(i)):
                    dve.wait_ge(table_hi_done, tables_split(i) + n + 1)
                    dve.tensor_tensor(table_lo[:, i % TABLE_RING, lo:hi], table_raw[:, i % TABLE_RING, lo:hi],
                                      table_hi[:, i % TABLE_RING, lo:hi].bitcast(f32),
                                      ALU.subtract).then_inc(table_lo_done, 1)

            dve.wait_ge(rows_numbered, len(row_numbers))
            for step in STEPS:
                kind, i = step[0], step[1]
                if kind == "hot":
                    dve.wait_ge(hot_ids_in[i % IDB_RING], 16 * (i // IDB_RING + 1))
                    for c in range(CHUNKS[i] - 1):
                        n = hot_before[i] + c
                        if n == FIRST_ONE_HOTS:
                            split_table(0)
                        if n >= HOT_RING:
                            dve.wait_ge(hot_used, n - HOT_RING + 1)
                        dve.tensor_scalar(one_hot[:, n % HOT_RING, :], hot_ids_b[:, i % IDB_RING, :],
                                          row_numbers[CHUNKS[i]][:, c:c + 1], None,
                                          ALU.is_equal).then_inc(hot_built, 1)
                    if i + 1 < N_HOT:
                        split_table(i + 1)
                elif kind == "x_lo":
                    dve.wait_ge(x_hi_done, 1)
                    dve.tensor_tensor(x_lo[:], x_t[:], x_hi[:].bitcast(f32), ALU.subtract).then_inc(x_lo_done, 1)
                elif kind == "dots":
                    m = step[2]
                    dve.wait_ge(dot_span_full, i * SPANS + m + 1)
                    if m == 0 and i == 0:
                        dve.wait_ge(pads_done, 3)
                    elif m == 0:
                        dve.wait_ge(pairs_lo_done, PARTS * i)
                    move_dots(dve.tensor_copy, i, m, (0, 1)).then_inc(moved_dve, 1)
                elif kind == "split":
                    for n, (lo, hi) in enumerate(PAIR_PARTS):
                        dve.wait_ge(pairs_hi_done, PARTS * i + n + 1)
                        dve.tensor_tensor(pairs_lo[:, i % 2, lo:hi, :], pairs[:, lo:hi, :],
                                          pairs_hi[:, i % 2, lo:hi, :].bitcast(f32),
                                          ALU.subtract).then_inc(pairs_lo_done, 1)
                elif kind == "pads":
                    dve.memset(pairs[:, 0, :], 1.0).then_inc(pads_done, 1)
                    dve.memset(pairs[:, 1:QCOLS, :], 0.0).then_inc(pads_done, 1)
                    dve.memset(one[:], 1.0).then_inc(one_done, 1)
                elif kind == "weights_lo":
                    dve.wait_ge(w1_hi_done, W_ORDER.index(i) + 1)
                    dve.tensor_tensor(w1_lo[:, i, :], w1_raw[:, W_PLACES[i], :], w1_hi[:, i, :].bitcast(f32),
                                      ALU.subtract).then_inc(w1_lo_done, 1)
                elif kind == "turn":
                    dve.wait_ge(h1t_full, i + 1)
                    if i >= 2:
                        dve.wait_ge(h2_full, i - 1)
                    dve.tensor_copy(h1_t[:, i % 2, :], ht_bank[:]).then_inc(h1t_done, 1)
                elif kind == "layer2":
                    if i == 0:
                        dve.wait_ge(b2_in, 16)
                        dve.wait_ge(w3_in, 16)
                    dve.wait_ge(h2_full, i + 1)
                    if i >= 1:
                        dve.wait_ge(y_done, i)
                    dve.tensor_tensor(h2[:], ht_bank[:, 0:H2], b2_b[:], ALU.add).then_inc(h2_done, 1)
                    dve.wait_ge(h2_done, i + 1)
                    dve.scalar_tensor_tensor(out=h2_w3[:], in0=h2[:], scalar=0.0, in1=w3_b[:], op0=ALU.max,
                                             op1=ALU.mult, accum_out=y[:, i:i + 1]).then_inc(y_done, 1)
                elif kind == "last_turn":
                    dve.wait_ge(h1t_full, TILES + i)
                    dve.wait_ge(h2_full, TILES - 2)
                    dve.tensor_copy(h1_t[:, (TILES - 1) % 2, i * HALF:(i + 1) * HALF],
                                    ht_halves[i][:, 0:HALF]).then_inc(h1t_done, 1)
                elif kind == "last_layer2" and i == 1:
                    dve.wait_ge(h2_full, TILES)
                    dve.wait_ge(y_done, TILES - 1)
                    dve.scalar_tensor_tensor(out=h2_w3[:], in0=ht_bank[:, 0:H2], scalar=0.0, in1=w3_b[:],
                                             op0=ALU.max, op1=ALU.mult,
                                             accum_out=y[:, TILES - 1:TILES]).then_inc(y_done, 1)

        @block.tensor
        def _(pe):
            def layer1(t, chunks, to, lo_col, hi_col):
                r = t % 2
                firsts = [first for first, _ in PAIR_PARTS]
                parts = [(x_hi[:, t * P:(t + 1) * P], x_lo[:, t * P:(t + 1) * P], QCOLS)]
                parts += [(pairs_hi[:, r, c, :], pairs_lo[:, r, c, :], c) for c in range(QCOLS)]
                for n in chunks:
                    hi, lo, c = parts[n]
                    if c in firsts:
                        pe.wait_ge(pairs_hi_done, PARTS * t + firsts.index(c) + 1)
                    if t == 0:
                        pe.wait_ge(w1_lo_done, n + 1)
                    pe.matmul(to, hi, w1_hi[:, c, lo_col:hi_col], start=(n == 0), stop=False)
                    pe.matmul(to, hi, w1_lo[:, c, lo_col:hi_col], start=False, stop=False)
                    if c in firsts:
                        pe.wait_ge(pairs_lo_done, PARTS * t + firsts.index(c) + 1)
                    last = pe.matmul(to, lo, w1_hi[:, c, lo_col:hi_col], start=False, stop=(n == len(parts) - 1))
                return last

            pe.wait_ge(ident_done, 1)
            for _ in range(WARM_UP):
                pe.transpose(slot_banks[0][:, 0:P], ident[:], ident[:])
            for step in STEPS:
                kind, i = step[0], step[1]
                if kind == "hot":
                    if i >= 2:
                        pe.wait_ge(hot_slot_filled, i - 1)
                    bank = hot_banks[i % 2]
                    r = i % TABLE_RING
                    for c in range(CHUNKS[i]):
                        m = hot_before[i] + c
                        for n, (lo, _) in enumerate(table_parts(i)):
                            if c * D == lo:
                                pe.wait_ge(table_lo_done, tables_split(i) + n + 1)
                        hots_built(pe, i, c)
                        pe.matmul(bank[:], table_hi[:, r, c * D:(c + 1) * D], one_hot[:, m % HOT_RING, :],
                                  start=(c == 0), stop=False)
                        last = pe.matmul(bank[:], table_lo[:, r, c * D:(c + 1) * D], one_hot[:, m % HOT_RING, :],
                                         start=False, stop=(c == CHUNKS[i] - 1))
                        last.then_inc(hot_used, 1)
                elif kind == "transpose":
                    lo, hi = GROUPS[step[2]]
                    n = group_no(i, step[2])
                    bank = slot_banks[n % 2]
                    if n >= 2:
                        pe.wait_ge(slots_filled, n - 1)
                    pe.wait_ge(rows_in[i % GATHER_RING][step[2]], 16 * (hi - lo) * (i // GATHER_RING + 1))
                    for m in range(hi - lo):
                        last = pe.transpose(bank[:, m * P:(m + 1) * P],
                                            gathered[:, i % GATHER_RING, lo + m, :], ident[:])
                    last.then_inc(transposed, 1)
                elif kind == "dots":
                    m = step[2]
                    n = i * SPANS + m
                    if m == 0:
                        pe.wait_ge(slots_filled, (i + 1) * n_groups)
                    if n == 0:
                        pe.wait_ge(hot_slot_filled, N_HOT)
                        pe.wait_ge(x_slot_done, 1)
                        pe.wait_ge(pads_done, 1)
                    if n >= 2:
                        pe.wait_ge(moved_dve, n - 1)
                        pe.wait_ge(moved_act, n - 1)
                    for g in range(SPAN_ROWS):
                        k = m * SPAN_ROWS + g
                        at = g // BANK_GROUPS * BANK + g % BANK_GROUPS * QUADS * COLS
                        last = pe.matmul(dot_spans[n % 2][:, at:at + QUADS * COLS],
                                         combined_t[:, i, k].rearrange("p j s -> p (j s)"),
                                         combined_t[:, i, k, :, 1:SLOTS],
                                         start=True, stop=True)
                    last.then_inc(dot_span_full, 1)
                elif kind == "layer1":
                    if i == 0:
                        pe.wait_ge(x_lo_done, 1)
                    else:
                        pe.wait_ge(h1_done, i)
                    last = layer1(i, range(*L1_PARTS[step[2]]), h_bank[:], 0, H1)
                    if step[2] == len(L1_PARTS) - 1:
                        last.then_inc(h1_full, 1)
                elif kind == "last_layer1":
                    if i == 0:
                        pe.wait_ge(h1_done, TILES - 1)
                    else:
                        pe.wait_ge(slots_filled, TILES * n_groups)
                    layer1(TILES - 1, range(W_CHUNKS), h_halves[i][:, 0:HALF], i * HALF, (i + 1) * HALF
                           ).then_inc(h1_full, 1)
                elif kind == "turn":
                    pe.wait_ge(h1_done, i + 1)
                    if i >= 1:
                        pe.wait_ge(h2_done, i)
                    for c in range(H1 // P):
                        last = pe.transpose(ht_bank[:, c * P:(c + 1) * P], h1[:, i % 2, c * P:(c + 1) * P], ident[:])
                    last.then_inc(h1t_full, 1)
                elif kind == "last_turn":
                    pe.wait_ge(h1_done, TILES + i)
                    if i == 0:
                        pe.wait_ge(slots_filled, TILES * n_groups)
                        pe.wait_ge(moved_dve, TILES * SPANS)
                        pe.wait_ge(moved_act, TILES * SPANS)
                    for c in range(HALF // P):
                        at = i * HALF + c * P
                        last = pe.transpose(ht_halves[i][:, c * P:(c + 1) * P],
                                            h1[:, (TILES - 1) % 2, at:at + P], ident[:])
                    last.then_inc(h1t_full, 1)
                elif kind == "layer2":
                    if i == 0:
                        pe.wait_ge(w2_in, 16)
                    pe.wait_ge(h1t_done, i + 1)
                    for c in range(H1 // P):
                        last = pe.matmul(ht_bank[:, 0:H2], h1_t[:, i % 2, c * P:(c + 1) * P], w2_sb[:, c, :],
                                         start=(c == 0), stop=(c == H1 // P - 1))
                    last.then_inc(h2_full, 1)
                elif kind == "last_bias":
                    pe.wait_ge(h2_done, TILES - 1)
                    pe.wait_ge(one_done, 1)
                    pe.wait_ge(b2_in, 16)
                    pe.matmul(ht_bank[:, 0:H2], one[:], b2_b[0:1, :], start=True, stop=False)
                elif kind == "last_layer2":
                    pe.wait_ge(h1t_done, TILES + i)
                    for c in range(i * HALF // P, (i + 1) * HALF // P):
                        last = pe.matmul(ht_bank[:, 0:H2], h1_t[:, (TILES - 1) % 2, c * P:(c + 1) * P],
                                         w2_sb[:, c, :], start=False, stop=(c == H1 // P - 1))
                    if i == 1:
                        last.then_inc(h2_full, 1)


def pair_row(f, g):
    f, g = min(f, g), max(f, g)
    return f * SLOTS - f * (f + 1) // 2 + g - f - 1


def kernel(**inputs):
    import numpy as np
    import concourse.bacc as bacc
    from concourse.bass_utils import run_bass_kernel_spmd

    a = {name: np.ascontiguousarray(x) for name, x in inputs.items()}
    w_pairs = np.zeros((P, QCOLS, H1), a["W_top1"].dtype)
    for g in range(1, SLOTS):
        q, c = divmod(g - 1, QCOLS)
        for f in range(g):
            w_pairs[q * QUAD + f, c] = a["W_top1"][pair_row(ORDER[f], ORDER[g])]
    w_pairs[SLOTS, 0] = a["b_top1"]
    arrays = {
        "ids": np.ascontiguousarray(a["ids"].reshape(TILES, P, FEATURES).transpose(1, 0, 2).reshape(P, -1)),
        "hot_ids": np.ascontiguousarray(a["ids"].T[ONE_HOT]),
        "dense_t": np.ascontiguousarray(a["r_dense_x"].T),
        "w_pairs": w_pairs.reshape(P, -1),
        "w_dense": np.ascontiguousarray(a["W_top1"][PAIRS:]),
        "w2": a["W_top2"],
        "b2": a["b_top2"].reshape(1, H2),
        "w3": a["W_top3"].reshape(1, H2),
    }
    for f in range(FEATURES):
        arrays[f"tbl_{f}"] = a[f"tbl_{f}"]
    nc = bacc.Bacc("TRN2", target_bir_lowering=False, num_devices=1)
    aps = {name: nc.dram_tensor(name, x.shape, mybir.dt.from_np(x.dtype), kind="ExternalInput").ap()
           for name, x in arrays.items()}
    out = nc.dram_tensor("out", (B, 1), mybir.dt.float32, kind="ExternalOutput").ap()
    dlrm_kernel(nc, aps["ids"], aps["hot_ids"], aps["dense_t"], [aps[f"tbl_{f}"] for f in range(FEATURES)],
                aps["w_pairs"], aps["w_dense"], aps["w2"], aps["b2"], aps["w3"], out)
    r = run_bass_kernel_spmd(nc, [arrays], core_ids=[0])
    return r.results[0]["out"]
```
